# Optimizing a Trainium2 kernel written in Bass

```python
import numpy as np
import jax
import jax.numpy as jnp

def _softmax(x, axis=-1):
    return jax.nn.softmax(x, axis=axis)

def _gelu(x):
    return jax.nn.gelu(x, approximate=True)

def _silu(x):
    return jax.nn.silu(x)

def _sigmoid(x):
    return jax.nn.sigmoid(x)

def _layernorm(x, axis=-1, eps=1e-05):
    m = jnp.mean(x, axis=axis, keepdims=True)
    v = jnp.var(x, axis=axis, keepdims=True)
    return (x - m) / jnp.sqrt(v + eps)

def _scatter_add(tgt, idx, src, axis=0):
    return tgt.at[idx].add(src)

def _segment_sum(src, seg, n):
    return jax.ops.segment_sum(src, seg, n)
kernel_name = 'mk_dlrm_tower_d1_rec_r8_b3b4ac'

def setup_inputs(seed: int=0):
    np.random.seed(seed)
    _w = jnp.asarray

    def _rec_inputs():
        import jax
        import jax.numpy as jnp
        _tk = jax.random.key(seed)
        dense_ctx = jax.random.normal(jax.random.fold_in(_tk, 190), (512, 16), jnp.float32)
        ids = jnp.stack([jax.random.randint(jax.random.fold_in(_tk, 200 + f), (512,), 0, v, jnp.int32) for f, v in enumerate([1000, 125000, 1250, 1000, 12500, 1000, 125000, 12500, 1250, 125000, 1250, 1250, 1250, 1000, 1000, 12500, 1250, 1250, 1250, 1250, 1250, 12500, 1250, 12500, 1250, 1000, 1250, 1000, 12500, 1250, 125000, 125000, 12500, 1250, 1250, 1000, 1250, 1000, 12500, 1250])], axis=1)
        tbl_0 = 0.05 * jax.random.normal(jax.random.fold_in(_tk, 500 + 0), (1000, 32), jnp.float32)
        tbl_1 = 0.05 * jax.random.normal(jax.random.fold_in(_tk, 500 + 1), (125000, 32), jnp.float32)
        tbl_2 = 0.05 * jax.random.normal(jax.random.fold_in(_tk, 500 + 2), (1250, 32), jnp.float32)
        tbl_3 = 0.05 * jax.random.normal(jax.random.fold_in(_tk, 500 + 3), (1000, 32), jnp.float32)
        tbl_4 = 0.05 * jax.random.normal(jax.random.fold_in(_tk, 500 + 4), (12500, 32), jnp.float32)
        tbl_5 = 0.05 * jax.random.normal(jax.random.fold_in(_tk, 500 + 5), (1000, 32), jnp.float32)
        tbl_6 = 0.05 * jax.random.normal(jax.random.fold_in(_tk, 500 + 6), (125000, 32), jnp.float32)
        tbl_7 = 0.05 * jax.random.normal(jax.random.fold_in(_tk, 500 + 7), (12500, 32), jnp.float32)
        tbl_8 = 0.05 * jax.random.normal(jax.random.fold_in(_tk, 500 + 8), (1250, 32), jnp.float32)
        tbl_9 = 0.05 * jax.random.normal(jax.random.fold_in(_tk, 500 + 9), (125000, 32), jnp.float32)
        tbl_10 = 0.05 * jax.random.normal(jax.random.fold_in(_tk, 500 + 10), (1250, 32), jnp.float32)
        tbl_11 = 0.05 * jax.random.normal(jax.random.fold_in(_tk, 500 + 11), (1250, 32), jnp.float32)
        tbl_12 = 0.05 * jax.random.normal(jax.random.fold_in(_tk, 500 + 12), (1250, 32), jnp.float32)
        tbl_13 = 0.05 * jax.random.normal(jax.random.fold_in(_tk, 500 + 13), (1000, 32), jnp.float32)
        tbl_14 = 0.05 * jax.random.normal(jax.random.fold_in(_tk, 500 + 14), (1000, 32), jnp.float32)
        tbl_15 = 0.05 * jax.random.normal(jax.random.fold_in(_tk, 500 + 15), (12500, 32), jnp.float32)
        tbl_16 = 0.05 * jax.random.normal(jax.random.fold_in(_tk, 500 + 16), (1250, 32), jnp.float32)
        tbl_17 = 0.05 * jax.random.normal(jax.random.fold_in(_tk, 500 + 17), (1250, 32), jnp.float32)
        tbl_18 = 0.05 * jax.random.normal(jax.random.fold_in(_tk, 500 + 18), (1250, 32), jnp.float32)
        tbl_19 = 0.05 * jax.random.normal(jax.random.fold_in(_tk, 500 + 19), (1250, 32), jnp.float32)
        tbl_20 = 0.05 * jax.random.normal(jax.random.fold_in(_tk, 500 + 20), (1250, 32), jnp.float32)
        tbl_21 = 0.05 * jax.random.normal(jax.random.fold_in(_tk, 500 + 21), (12500, 32), jnp.float32)
        tbl_22 = 0.05 * jax.random.normal(jax.random.fold_in(_tk, 500 + 22), (1250, 32), jnp.float32)
        tbl_23 = 0.05 * jax.random.normal(jax.random.fold_in(_tk, 500 + 23), (12500, 32), jnp.float32)
        tbl_24 = 0.05 * jax.random.normal(jax.random.fold_in(_tk, 500 + 24), (1250, 32), jnp.float32)
        tbl_25 = 0.05 * jax.random.normal(jax.random.fold_in(_tk, 500 + 25), (1000, 32), jnp.float32)
        tbl_26 = 0.05 * jax.random.normal(jax.random.fold_in(_tk, 500 + 26), (1250, 32), jnp.float32)
        tbl_27 = 0.05 * jax.random.normal(jax.random.fold_in(_tk, 500 + 27), (1000, 32), jnp.float32)
        tbl_28 = 0.05 * jax.random.normal(jax.random.fold_in(_tk, 500 + 28), (12500, 32), jnp.float32)
        tbl_29 = 0.05 * jax.random.normal(jax.random.fold_in(_tk, 500 + 29), (1250, 32), jnp.float32)
        tbl_30 = 0.05 * jax.random.normal(jax.random.fold_in(_tk, 500 + 30), (125000, 32), jnp.float32)
        tbl_31 = 0.05 * jax.random.normal(jax.random.fold_in(_tk, 500 + 31), (125000, 32), jnp.float32)
        tbl_32 = 0.05 * jax.random.normal(jax.random.fold_in(_tk, 500 + 32), (12500, 32), jnp.float32)
        tbl_33 = 0.05 * jax.random.normal(jax.random.fold_in(_tk, 500 + 33), (1250, 32), jnp.float32)
        tbl_34 = 0.05 * jax.random.normal(jax.random.fold_in(_tk, 500 + 34), (1250, 32), jnp.float32)
        tbl_35 = 0.05 * jax.random.normal(jax.random.fold_in(_tk, 500 + 35), (1000, 32), jnp.float32)
        tbl_36 = 0.05 * jax.random.normal(jax.random.fold_in(_tk, 500 + 36), (1250, 32), jnp.float32)
        tbl_37 = 0.05 * jax.random.normal(jax.random.fold_in(_tk, 500 + 37), (1000, 32), jnp.float32)
        tbl_38 = 0.05 * jax.random.normal(jax.random.fold_in(_tk, 500 + 38), (12500, 32), jnp.float32)
        tbl_39 = 0.05 * jax.random.normal(jax.random.fold_in(_tk, 500 + 39), (1250, 32), jnp.float32)
        _rk = jax.random.fold_in(_tk, 7)
        W_top1 = 0.176777 * jax.random.normal(jax.random.fold_in(_tk, 801), (32, 512), jnp.float32)
        W_top2 = 0.0441942 * jax.random.normal(jax.random.fold_in(_tk, 802), (512, 256), jnp.float32)
        W_top3 = 0.0625 * jax.random.normal(jax.random.fold_in(_tk, 803), (256, 1), jnp.float32)
        b_top1 = jnp.zeros((512,), jnp.float32)
        b_top2 = jnp.zeros((256,), jnp.float32)
        return (dense_ctx, ids, tbl_0, tbl_1, tbl_2, tbl_3, tbl_4, tbl_5, tbl_6, tbl_7, tbl_8, tbl_9, tbl_10, tbl_11, tbl_12, tbl_13, tbl_14, tbl_15, tbl_16, tbl_17, tbl_18, tbl_19, tbl_20, tbl_21, tbl_22, tbl_23, tbl_24, tbl_25, tbl_26, tbl_27, tbl_28, tbl_29, tbl_30, tbl_31, tbl_32, tbl_33, tbl_34, tbl_35, tbl_36, tbl_37, tbl_38, tbl_39, W_top1, b_top1, W_top2, b_top2, W_top3)
    dense_ctx, ids, tbl_0, tbl_1, tbl_2, tbl_3, tbl_4, tbl_5, tbl_6, tbl_7, tbl_8, tbl_9, tbl_10, tbl_11, tbl_12, tbl_13, tbl_14, tbl_15, tbl_16, tbl_17, tbl_18, tbl_19, tbl_20, tbl_21, tbl_22, tbl_23, tbl_24, tbl_25, tbl_26, tbl_27, tbl_28, tbl_29, tbl_30, tbl_31, tbl_32, tbl_33, tbl_34, tbl_35, tbl_36, tbl_37, tbl_38, tbl_39, W_top1, b_top1, W_top2, b_top2, W_top3 = _rec_inputs()

    def _L0_rec_setup():
        import jax, jax.numpy as jnp
        import numpy as np
        import itertools
        LN_EPS = 0.001

        def _pair_indices(field_num):
            pairs = np.array(list(itertools.combinations(range(field_num), 2)), dtype=np.int32)
            return (pairs[:, 0], pairs[:, 1])
        key = jax.random.key(seed)
        ks = jax.random.split(key, 3)
        B, F, E, P, D = (256, 40, 32, 780, 16)
        x = jax.random.normal(ks[0], (B, F, E), dtype=jnp.float32)
        W = jax.random.normal(ks[1], (P, E, E), dtype=jnp.float32) * (2.0 / (E + E)) ** 0.5
        dense_w = jax.random.normal(ks[2], (P, D), dtype=jnp.float32) * (2.0 / (P + D)) ** 0.5
        dense_b = jnp.zeros((D,), dtype=jnp.float32)
        gamma = jnp.ones((D,), dtype=jnp.float32)
        beta = jnp.zeros((D,), dtype=jnp.float32)
        return {'x': x, 'W': W, 'dense_w': dense_w, 'dense_b': dense_b, 'gamma': gamma, 'beta': beta}
    _L0_rec_all = _L0_rec_setup()
    _L0_rec_in = {k: v for k, v in _L0_rec_all.items() if k in ('W', 'dense_w', 'dense_b', 'gamma', 'beta')}
    del _L0_rec_all
    return {'dense_ctx': dense_ctx, 'ids': ids, 'tbl_0': tbl_0, 'tbl_1': tbl_1, 'tbl_2': tbl_2, 'tbl_3': tbl_3, 'tbl_4': tbl_4, 'tbl_5': tbl_5, 'tbl_6': tbl_6, 'tbl_7': tbl_7, 'tbl_8': tbl_8, 'tbl_9': tbl_9, 'tbl_10': tbl_10, 'tbl_11': tbl_11, 'tbl_12': tbl_12, 'tbl_13': tbl_13, 'tbl_14': tbl_14, 'tbl_15': tbl_15, 'tbl_16': tbl_16, 'tbl_17': tbl_17, 'tbl_18': tbl_18, 'tbl_19': tbl_19, 'tbl_20': tbl_20, 'tbl_21': tbl_21, 'tbl_22': tbl_22, 'tbl_23': tbl_23, 'tbl_24': tbl_24, 'tbl_25': tbl_25, 'tbl_26': tbl_26, 'tbl_27': tbl_27, 'tbl_28': tbl_28, 'tbl_29': tbl_29, 'tbl_30': tbl_30, 'tbl_31': tbl_31, 'tbl_32': tbl_32, 'tbl_33': tbl_33, 'tbl_34': tbl_34, 'tbl_35': tbl_35, 'tbl_36': tbl_36, 'tbl_37': tbl_37, 'tbl_38': tbl_38, 'tbl_39': tbl_39, 'W_top1': W_top1, 'b_top1': b_top1, 'W_top2': W_top2, 'b_top2': b_top2, 'W_top3': W_top3, 'L0_rec_W': _L0_rec_in['W'], 'L0_rec_dense_w': _L0_rec_in['dense_w'], 'L0_rec_dense_b': _L0_rec_in['dense_b'], 'L0_rec_gamma': _L0_rec_in['gamma'], 'L0_rec_beta': _L0_rec_in['beta']}

def reference(dense_ctx, ids, tbl_0, tbl_1, tbl_2, tbl_3, tbl_4, tbl_5, tbl_6, tbl_7, tbl_8, tbl_9, tbl_10, tbl_11, tbl_12, tbl_13, tbl_14, tbl_15, tbl_16, tbl_17, tbl_18, tbl_19, tbl_20, tbl_21, tbl_22, tbl_23, tbl_24, tbl_25, tbl_26, tbl_27, tbl_28, tbl_29, tbl_30, tbl_31, tbl_32, tbl_33, tbl_34, tbl_35, tbl_36, tbl_37, tbl_38, tbl_39, W_top1, b_top1, W_top2, b_top2, W_top3, L0_rec_W, L0_rec_dense_w, L0_rec_dense_b, L0_rec_gamma, L0_rec_beta):
    import jax
    import jax.numpy as jnp

    def _L0_rec_ref(x, W, dense_w, dense_b, gamma, beta):
        import jax, jax.numpy as jnp
        import numpy as np
        import itertools
        LN_EPS = 0.001

        def _pair_indices(field_num):
            pairs = np.array(list(itertools.combinations(range(field_num), 2)), dtype=np.int32)
            return (pairs[:, 0], pairs[:, 1])
        F = x.shape[1]
        idx_i, idx_j = _pair_indices(F)
        xi = x[:, idx_i, :]
        xj = x[:, idx_j, :]
        t = jnp.einsum('bpe,pef->bpf', xi, W)
        p = jnp.einsum('bpf,bpf->bp', t, xj)
        h = p @ dense_w + dense_b
        mu = jnp.mean(h, axis=-1, keepdims=True)
        var = jnp.mean(jnp.square(h - mu), axis=-1, keepdims=True)
        out = (h - mu) * jax.lax.rsqrt(var + LN_EPS) * gamma + beta
        return out
    e = jnp.stack([tbl_0[ids[:, 0]], tbl_1[ids[:, 1]], tbl_2[ids[:, 2]], tbl_3[ids[:, 3]], tbl_4[ids[:, 4]], tbl_5[ids[:, 5]], tbl_6[ids[:, 6]], tbl_7[ids[:, 7]], tbl_8[ids[:, 8]], tbl_9[ids[:, 9]], tbl_10[ids[:, 10]], tbl_11[ids[:, 11]], tbl_12[ids[:, 12]], tbl_13[ids[:, 13]], tbl_14[ids[:, 14]], tbl_15[ids[:, 15]], tbl_16[ids[:, 16]], tbl_17[ids[:, 17]], tbl_18[ids[:, 18]], tbl_19[ids[:, 19]], tbl_20[ids[:, 20]], tbl_21[ids[:, 21]], tbl_22[ids[:, 22]], tbl_23[ids[:, 23]], tbl_24[ids[:, 24]], tbl_25[ids[:, 25]], tbl_26[ids[:, 26]], tbl_27[ids[:, 27]], tbl_28[ids[:, 28]], tbl_29[ids[:, 29]], tbl_30[ids[:, 30]], tbl_31[ids[:, 31]], tbl_32[ids[:, 32]], tbl_33[ids[:, 33]], tbl_34[ids[:, 34]], tbl_35[ids[:, 35]], tbl_36[ids[:, 36]], tbl_37[ids[:, 37]], tbl_38[ids[:, 38]], tbl_39[ids[:, 39]]], axis=1)
    z = _L0_rec_ref(e, L0_rec_W, L0_rec_dense_w, L0_rec_dense_b, L0_rec_gamma, L0_rec_beta)
    z = z.reshape(z.shape[0], -1)
    h = jnp.concatenate([z, dense_ctx], axis=1)
    h = jnp.maximum(h @ W_top1 + b_top1, 0.0)
    h = jnp.maximum(h @ W_top2 + b_top2, 0.0)
    y = h @ W_top3
    return y

_drawn_inputs = setup_inputs


def setup_inputs(seed=0):
    import zlib

    import numpy as np

    out = dict(_drawn_inputs(seed))
    spreads = {'b_top1': (0.0, 0.1),
     'b_top2': (0.0, 0.1),
     'L0_rec_dense_b': (0.0, 0.1),
     'L0_rec_gamma': (1.0, 0.2),
     'L0_rec_beta': (0.0, 0.1)}
    factors = {}
    for name, (base, spread) in spreads.items():
        noise = np.random.default_rng([zlib.crc32(name.encode()), seed]).standard_normal(out[name].shape)
        drawn = base * np.exp(spread * noise) if base else spread * noise
        out[name] = jnp.asarray(drawn.astype(out[name].dtype))
    for name, factor in factors.items():
        out[name] = (out[name] * factor).astype(out[name].dtype)
    return out
```

```python
import numpy as np
import concourse.bass as bass
from concourse import mybir
from contextlib import ExitStack

B, F, E, D = 512, 40, 32, 16
CTX = 16
N1, N2 = 512, 256
LN_EPS = 0.001
P = 128
BT = B // P
R = P // E
G = F // R
ROWS_OF = [sum(range(1, j + 1)) for j in range(G)]
NBR = G * (G + 1) // 2


def build(nc, ids, tables, w_nat, w_dense, dense_b, gamma, beta, ctx_in, w1, b1, w2, b2, w3,
          ident_in, sel_in, out):
    fp32, i32 = mybir.dt.float32, mybir.dt.int32
    ALU, ACT, AX = mybir.AluOpType, mybir.ActivationFunctionType, mybir.AxisListType

    with ExitStack() as ctx:
        def sb(name, shape, dt=fp32):
            return ctx.enter_context(nc.sbuf_tensor(name, shape, dt))

        def pb(name, shape, dt=fp32):
            return ctx.enter_context(nc.psum_tensor(name, shape, dt))

        def sem(name):
            return ctx.enter_context(nc.semaphore(name))

        ids_sb = sb("ids_sb", [P, F, BT], i32)
        emb = sb("emb", [P, 2, BT, R, E])
        xT = sb("xT", [P, G, B])
        w_sb = sb("w_sb", [P, 2, G, P])
        wd_sb = sb("wd_sb", [P, NBR * R, D])
        prod = sb("prod", [P, 3, R, B])
        ident = sb("ident", [P, P])
        sel = sb("sel", [P, D])
        hT = sb("hT", [P, B])
        ones = sb("ones", [1, P])
        db_sb = sb("db_sb", [1, D])
        gcol = sb("gcol", [D + CTX, 1])
        bcol = sb("bcol", [D + CTX, 1])
        w1_sb = sb("w1_sb", [D + CTX, N1])
        b1_sb = sb("b1_sb", [P, N1 // P])
        w2_sb = sb("w2_sb", [P, N1 // P, N2])
        b2_sb = sb("b2_sb", [P, N2 // P])
        w3_sb = sb("w3_sb", [P, N2 // P])
        h_sb = sb("h_sb", [P, BT, D])
        sq = sb("sq", [P, BT, D])
        stat = sb("stat", [P, 4, BT])
        eps = sb("eps", [P, 1])
        warm = sb("warm", [P, 1])
        cat = sb("cat", [P, BT, D + CTX])
        catT = sb("catT", [D + CTX, B])
        a1 = sb("a1", [P, N1 // P, B])
        a2 = sb("a2", [P, N2 // P, B])
        y_sb = sb("y_sb", [1, B])

        t_ps = [pb(f"t_ps{i}", [P, 2, B]) for i in range(2)]
        hT_ps = pb("hT_ps", [P, B])
        x_ps = pb("x_ps", [P, B])
        m_ps = [pb(f"m_ps{i}", [P, B]) for i in range(2)]

        ids_in = sem("ids_in")
        gathered = [sem(f"gathered{j}") for j in range(G)]
        w_in = [sem(f"w_in{i}") for i in range(2)]
        consts_in = sem("consts_in")
        memset_done = sem("memset_done")
        x_turned = sem("x_turned")
        x_kept = sem("x_kept")
        t_ready = sem("t_ready")
        prod_ready = sem("prod_ready")
        summed = sem("summed")
        top_in = sem("top_in")
        h_copied = sem("h_copied")
        hb_ready = sem("hb_ready")
        ln = sem("ln")
        std_ready = sem("std_ready")
        cat_ready = sem("cat_ready")
        cat_turned = sem("cat_turned")
        catT_ready = sem("catT_ready")
        l1_ready = sem("l1_ready")
        a1_ready = sem("a1_ready")
        l2_ready = sem("l2_ready")
        a2_ready = sem("a2_ready")
        y_ready = sem("y_ready")
        y_kept = sem("y_kept")
        stored = sem("stored")

        block = ctx.enter_context(nc.Block())

        steps = [(J, I) for J in range(G) for I in range(J + 1)]
        width = {s: R if s[1] < s[0] else R - 1 for s in steps}
        NH = 2 * len(steps)

        @block.sync
        def _(sp):
            sp.dma_start(ids_sb[:], ids).then_inc(ids_in, 16)
            sp.dma_start(ident[:], ident_in).then_inc(consts_in, 16)
            for j in range(R):
                sp.dma_start(wd_sb[j * E:(j + 1) * E].rearrange("p k d -> p (k d)"),
                             w_dense[j:j + 1, :].to_broadcast([E, NBR * R * D])).then_inc(consts_in, 16)
            for J in range(G):
                if J >= 2:
                    sp.wait_ge(t_ready, 2 * ROWS_OF[J - 1])
                sp.dma_start(w_sb[:, J % 2, 0:J + 1, :],
                             w_nat[:, ROWS_OF[J] * P:(ROWS_OF[J] + J + 1) * P]
                             .rearrange("p (i c) -> p i c", c=P)).then_inc(w_in[J % 2], 16)
                if J == 1:
                    sp.wait_ge(memset_done, 1)
                    for dst, src in ((sel[:], sel_in), (db_sb[:], dense_b), (gcol[0:D], gamma),
                                     (bcol[0:D], beta), (w1_sb[:], w1), (b1_sb[:], b1),
                                     (w2_sb[:], w2.rearrange("(k p) n -> p k n", p=P)), (b2_sb[:], b2),
                                     (w3_sb[:], w3),
                                     (cat[:, :, D:], ctx_in.rearrange("(t p) c -> p t c", p=P))):
                        sp.dma_start(dst, src).then_inc(top_in, 16)
            sp.wait_ge(y_kept, 1)
            sp.dma_start(out, y_sb[:]).then_inc(stored, 16)
            sp.wait_ge(stored, 16)

        CONSTS1 = 16 * (1 + R)
        CONSTS = 16 * 10

        @block.gpsimd
        def _(pool):
            pool.wait_ge(ids_in, 16)
            for J in range(G):
                if J >= 2:
                    pool.wait_ge(x_turned, J - 1)
                for t in range(BT):
                    for r in range(R):
                        f = J * R + r
                        pool.indirect_dma_start(
                            emb[:, J % 2, t, r, :], None, tables[f],
                            bass.IndirectOffsetOnAxis(ap=ids_sb[:, f, t:t + 1], axis=0),
                        ).then_inc(gathered[J], 16)

        @block.scalar
        def _(act):
            act.wait_ge(memset_done, 1)
            act.activation(warm[:], eps[:], ACT.Sqrt)
            for J in range(G):
                act.wait_ge(x_turned, J + 1)
                act.activation(xT[:, J, :], x_ps[:], ACT.Copy).then_inc(x_kept, 1)
            act.wait_ge(summed, len(steps))
            for c in range(2):
                act.activation(hT[c * E:c * E + D, :], hT_ps[c * E:c * E + D, :], ACT.Copy).then_inc(h_copied, 1)
            act.wait_ge(ln, 4)
            act.activation(stat[:, 2, :], stat[:, 1, :], ACT.Sqrt, bias=eps[:], scale=1.0 / D).then_inc(std_ready, 1)
            act.wait_ge(cat_turned, 1)
            act.wait_ge(top_in, CONSTS)
            act.activation(catT[:], x_ps[0:D + CTX, :], ACT.Identity, bias=bcol[:], scale=gcol[:]).then_inc(catT_ready, 1)
            for c in range(N1 // P):
                act.wait_ge(l1_ready, c + 1)
                act.activation(a1[:, c, :], m_ps[c % 2][:], ACT.Relu, bias=b1_sb[:, c:c + 1]).then_inc(a1_ready, 1)
            for c in range(N2 // P):
                act.wait_ge(l2_ready, c + 1)
                act.activation(a2[:, c, :], m_ps[c % 2][:], ACT.Relu, bias=b2_sb[:, c:c + 1]).then_inc(a2_ready, 1)
            act.wait_ge(y_ready, 1)
            act.activation(y_sb[:], x_ps[0:1, :], ACT.Copy).then_inc(y_kept, 1)

        @block.vector
        def _(dve):
            dve.memset(hT[:], 0.0)
            dve.memset(ones[:], 1.0)
            dve.memset(gcol[:], 1.0)
            dve.memset(bcol[:], 0.0)
            dve.memset(eps[:], LN_EPS).then_inc(memset_done, 1)
            h = 0
            for s, (J, I) in enumerate(steps):
                for half in range(2):
                    n = min(2, width[J, I] - 2 * half)
                    dve.wait_ge(t_ready, h + 1)
                    if half == 0 and I == 0:
                        dve.wait_ge(x_kept, J + 1)
                    if half == 0 and s >= 3:
                        dve.wait_ge(summed, s - 2)
                    dve.tensor_tensor(
                        prod[:, s % 3, 2 * half:2 * half + n, :], t_ps[h % 2][:, 0:n, :],
                        xT[:, J:J + 1, :].to_broadcast([P, n, B]), ALU.mult).then_inc(prod_ready, 1)
                    h += 1
            dve.wait_ge(summed, len(steps))
            for c in range(2, R):
                dve.tensor_copy(hT[c * E:c * E + D, :], hT_ps[c * E:c * E + D, :]).then_inc(h_copied, 1)
            dve.wait_ge(hb_ready, 1)
            hb = m_ps[0][:, 0:BT * D].rearrange("p (t d) -> p t d", d=D)
            dve.tensor_reduce(stat[:, 0, :], hb, AX.X, ALU.add).then_inc(ln, 1)
            dve.wait_ge(ln, 1)
            dve.tensor_scalar(stat[:, 3, :], stat[:, 0, :], 1.0 / D, None, ALU.mult).then_inc(ln, 1)
            dve.wait_ge(ln, 2)
            dve.tensor_tensor(h_sb[:], hb, stat[:, 3, :].unsqueeze(2).to_broadcast([P, BT, D]), ALU.subtract).then_inc(ln, 1)
            dve.wait_ge(ln, 3)
            dve.tensor_tensor(sq[:], h_sb[:], h_sb[:], ALU.mult).then_inc(cat_ready, 1)
            dve.wait_ge(cat_ready, 1)
            dve.tensor_reduce(stat[:, 1, :], sq[:], AX.X, ALU.add).then_inc(ln, 1)
            dve.wait_ge(std_ready, 1)
            dve.reciprocal(stat[:, 0, :], stat[:, 2, :]).then_inc(ln, 1)
            dve.wait_ge(ln, 5)
            dve.tensor_tensor(cat[:, :, 0:D], h_sb[:], stat[:, 0, :].unsqueeze(2).to_broadcast([P, BT, D]), ALU.mult).then_inc(cat_ready, 1)

        @block.tensor
        def _(pe):
            h = 0
            opened = set()

            def reduce_step(s):
                J, I = steps[s]
                pe.wait_ge(prod_ready, 2 * (s + 1))
                for q in range(width[J, I]):
                    final = (s == len(steps) - 1) if q < R - 1 else (s == len(steps) - 2)
                    last = pe.matmul(hT_ps[q * E:q * E + D, :], wd_sb[:, s * R + q, :], prod[:, s % 3, q, :],
                                     start=q not in opened, stop=final)
                    opened.add(q)
                last.then_inc(summed, 1)

            pe.wait_ge(consts_in, CONSTS1)
            for s, (J, I) in enumerate(steps):
                if I == 0:
                    pe.wait_ge(gathered[J], 16 * R * BT)
                    if J >= 1:
                        pe.wait_ge(x_kept, J)
                    for t in range(BT):
                        last = pe.transpose(x_ps[:, t * P:(t + 1) * P],
                                            emb[:, J % 2, t, :, :].rearrange("p r e -> p (r e)"), ident[:])
                    last.then_inc(x_turned, 1)
                    pe.wait_ge(x_kept, J + 1)
                    pe.wait_ge(w_in[J % 2], 16 * (J // 2 + 1))
                for half in range(2):
                    n = min(2, width[J, I] - 2 * half)
                    if h >= 2:
                        pe.wait_ge(prod_ready, h - 1)
                    for k in range(n):
                        q = 2 * half + k
                        last = pe.matmul(t_ps[h % 2][:, k, :], w_sb[q * E:(q + 1) * E, J % 2, I, :],
                                         xT[q * E:(q + 1) * E, I, :], start=True, stop=True)
                    last.then_inc(t_ready, 1)
                    h += 1
                if s >= 1:
                    reduce_step(s - 1)
            reduce_step(len(steps) - 1)
            pe.wait_ge(h_copied, R)
            pe.wait_ge(top_in, CONSTS)
            for t in range(BT):
                o = m_ps[0][:, t * D:(t + 1) * D]
                pe.matmul(o, hT[:, t * P:(t + 1) * P], sel[:], start=True, stop=False)
                last = pe.matmul(o, ones[:], db_sb[:], start=False, stop=True)
            last.then_inc(hb_ready, 1)
            pe.wait_ge(cat_ready, 2)
            for t in range(BT):
                last = pe.transpose(x_ps[0:D + CTX, t * P:(t + 1) * P], cat[:, t, :], ident[:])
            last.then_inc(cat_turned, 1)
            pe.wait_ge(catT_ready, 1)
            for c in range(N1 // P):
                if c >= 2:
                    pe.wait_ge(a1_ready, c - 1)
                pe.matmul(m_ps[c % 2][:], w1_sb[:, c * P:(c + 1) * P], catT[:], start=True, stop=True).then_inc(l1_ready, 1)
            pe.wait_ge(a1_ready, N1 // P)
            for c in range(N2 // P):
                for k in range(N1 // P):
                    last = pe.matmul(m_ps[c % 2][:], w2_sb[:, k, c * P:(c + 1) * P], a1[:, k, :],
                                     start=k == 0, stop=k == N1 // P - 1)
                last.then_inc(l2_ready, 1)
            for k in range(N2 // P):
                pe.wait_ge(a2_ready, k + 1)
                last = pe.matmul(x_ps[0:1, :], w3_sb[:, k:k + 1], a2[:, k, :], start=k == 0, stop=k == N2 // P - 1)
            last.then_inc(y_ready, 1)


def kernel(**inputs):
    import concourse.bacc as bacc
    from concourse.bass_utils import run_bass_kernel_spmd

    a = {k: np.ascontiguousarray(v) for k, v in inputs.items()}
    arrays = {}
    arrays["ids"] = np.ascontiguousarray(a["ids"].reshape(BT, P, F).transpose(1, 2, 0).astype(np.int32, copy=False))
    for f in range(F):
        arrays[f"tbl_{f}"] = a[f"tbl_{f}"]
    pair = np.full((F, F), -1)
    pair[np.triu_indices(F, 1)] = np.arange(F * (F - 1) // 2)
    w_nat = np.zeros((R, E, NBR, R, E), a["L0_rec_W"].dtype)
    w_dense = np.zeros((R, NBR, R, D), a["L0_rec_dense_w"].dtype)
    for J in range(G):
        for I in range(J + 1):
            for q in range(R):
                for r in range(R):
                    p = pair[I * R + q, J * R + r]
                    if p >= 0:
                        w_nat[q, :, ROWS_OF[J] + I, r, :] = a["L0_rec_W"][p]
                        w_dense[r, ROWS_OF[J] + I, q, :] = a["L0_rec_dense_w"][p]
    arrays["w_nat"] = w_nat.reshape(P, NBR * P)
    arrays["w_dense"] = w_dense.reshape(R, NBR * R * D)
    arrays["dense_b"] = a["L0_rec_dense_b"].reshape(1, D)
    arrays["gamma"] = a["L0_rec_gamma"].reshape(D, 1)
    arrays["beta"] = a["L0_rec_beta"].reshape(D, 1)
    arrays["ctx_in"] = a["dense_ctx"]
    arrays["w1"] = a["W_top1"]
    arrays["b1"] = np.ascontiguousarray(a["b_top1"].reshape(N1 // P, P).T)
    arrays["w2"] = a["W_top2"]
    arrays["b2"] = np.ascontiguousarray(a["b_top2"].reshape(N2 // P, P).T)
    arrays["w3"] = np.ascontiguousarray(a["W_top3"].reshape(N2 // P, P).T)
    arrays["ident_in"] = np.eye(P, dtype=np.float32)
    arrays["sel_in"] = np.concatenate([np.eye(E, D, dtype=np.float32)] * R, axis=0)

    nc = bacc.Bacc("TRN2", target_bir_lowering=False, num_devices=1)
    ap = {n: nc.dram_tensor(n, v.shape, mybir.dt.from_np(v.dtype), kind="ExternalInput").ap() for n, v in arrays.items()}
    out = nc.dram_tensor("out", (B, 1), mybir.dt.float32, kind="ExternalOutput").ap()
    tables = [ap.pop(f"tbl_{f}") for f in range(F)]
    build(nc, tables=tables, out=out.rearrange("b o -> o b"), **ap)
    r = run_bass_kernel_spmd(nc, [arrays], core_ids=[0])
    return r.results[0]["out"]
```

```python
import numpy as np
import concourse.bass as bass
from concourse import mybir
from contextlib import ExitStack

B, F, E, D = 512, 40, 32, 16
CTX = 16
N1, N2 = 512, 256
LN_EPS = 0.001
P = 128
BT = B // P
R = P // E
G = F // R
ROWS_OF = [sum(range(1, j + 1)) for j in range(G)]
NBR = G * (G + 1) // 2
HALVES = 2
BH = B // HALVES
TH = BH // P
CR = 5
NC = -(-NBR // CR)
HIGH_BITS = 0xFFFFF000


def build(nc, ids, tables, w_nat, w_dense, dense_b, gamma, beta, ctx_in, w1, b1, w2, b2, w3,
          ident_in, sel_in, out):
    fp32, f32r, i32, u32 = mybir.dt.float32, mybir.dt.float32r, mybir.dt.int32, mybir.dt.uint32
    ALU, ACT, AX = mybir.AluOpType, mybir.ActivationFunctionType, mybir.AxisListType

    with ExitStack() as ctx:
        def sb(name, shape, dt=fp32):
            return ctx.enter_context(nc.sbuf_tensor(name, shape, dt))

        def pb(name, shape, dt=fp32):
            return ctx.enter_context(nc.psum_tensor(name, shape, dt))

        def sem(name):
            return ctx.enter_context(nc.semaphore(name))

        w_stack = sb("w_stack", [P, R, NBR, P], f32r)
        x_stack = sb("x_stack", [P, G, R, BH], f32r)
        xT = sb("xT", [P, 3, BH])
        emb = sb("emb", [P, 3, TH, R, E])
        emb_high = sb("emb_high", [P, TH, R, E])
        emb_parts = sb("emb_parts", [P, 2, TH, R, 2, 2, E], f32r)
        wd_sb = sb("wd_sb", [P, NBR * R, D])
        prod = sb("prod", [P, 2, R, BH])
        ids_sb = sb("ids_sb", [P, F, BT], i32)
        ident = sb("ident", [P, P])
        ident_r = sb("ident_r", [P, P], f32r)
        early = sb("early", [P, 5 * CR * P])
        w_low = early[:, 0:3 * CR * P].rearrange("p (u c) -> p u c", u=3)
        w_high = early[:, 3 * CR * P:].rearrange("p (u c) -> p u c", u=2)
        w2_sb = early[:, 0:N1 // P * N2].rearrange("p (k n) -> p k n", n=N2)
        a1 = early[:, N1 // P * N2:N1 // P * (N2 + BH)].rearrange("p (k b) -> p k b", b=BH)
        a2 = early[:, N1 // P * (N2 + BH):N1 // P * (N2 + BH) + N2 // P * BH].rearrange("p (k b) -> p k b", b=BH)
        hT = early[:, 4 * CR * P:4 * CR * P + BH]
        catT = early[0:D + CTX, 4 * CR * P + BH:4 * CR * P + 2 * BH]
        w1_sb = sb("w1_sb", [D + CTX, N1])
        sel = sb("sel", [P, D])
        ones = sb("ones", [1, P])
        db_sb = sb("db_sb", [1, D])
        gcol = sb("gcol", [D + CTX, 1])
        bcol = sb("bcol", [D + CTX, 1])
        b1_sb = sb("b1_sb", [P, N1 // P])
        b2_sb = sb("b2_sb", [P, N2 // P])
        w3_sb = sb("w3_sb", [P, N2 // P])
        h_sb = sb("h_sb", [P, TH, D])
        sq = sb("sq", [P, TH, D])
        total = sb("total", [P, TH])
        mean = sb("mean", [P, TH])
        var = sb("var", [P, TH])
        std = sb("std", [P, TH])
        rstd = sb("rstd", [P, TH])
        eps = sb("eps", [P, 1])
        warm = sb("warm", [P, 1])
        cat = sb("cat", [P, BT, D + CTX])
        y_sb = sb("y_sb", [1, BH])

        t_ps = [pb(f"t_ps{i}", [P, R, BH]) for i in range(2)]
        hT_ps = pb("hT_ps", [P, HALVES, BH])
        x_ps = [pb(f"x_ps{i}", [P, 2, BH]) for i in range(2)]
        top_ps = pb("top_ps", [P, BH])

        ids_in = sem("ids_in")
        gathered = [sem(f"gathered{g}") for g in range(HALVES * G)]
        w_in = [sem(f"w_in{i}") for i in range(3)]
        w_high_ready = sem("w_high_ready")
        w_split = sem("w_split")
        w_stacked = [sem(f"w_stacked{c}") for c in range(NC)]
        ident_kept = sem("ident_kept")
        ident_in_sb = sem("ident_in_sb")
        consts_in = sem("consts_in")
        top_in = sem("top_in")
        memset_done = sem("memset_done")
        high_ready = sem("high_ready")
        x_split = sem("x_split")
        x_doubled = sem("x_doubled")
        filled = sem("filled")
        kept = sem("kept")
        t_ready = sem("t_ready")
        prod_ready = sem("prod_ready")
        summed = sem("summed")
        h_copied = sem("h_copied")
        hb_ready = sem("hb_ready")
        ln = sem("ln")
        var_ready = sem("var_ready")
        std_ready = sem("std_ready")
        cat_ready = sem("cat_ready")
        cat_turned = sem("cat_turned")
        catT_ready = sem("catT_ready")
        l1_ready = sem("l1_ready")
        a1_ready = sem("a1_ready")
        l2_ready = sem("l2_ready")
        a2_ready = sem("a2_ready")
        y_ready = sem("y_ready")
        y_kept = sem("y_kept")
        stored = sem("stored")

        block = ctx.enter_context(nc.Block())

        NG = HALVES * G
        NS = HALVES * NBR

        FILLS = R // 2 + 1

        def split_at(J):
            return max(0, J - 3)

        def fill_at(J, k):
            return max(0, J - 2 + k)

        STACK_INC = 16 * 4 * R

        CONSTS = 16 * R
        TOP = 16 * 10

        def blocks(I, J):
            return R if I < J else R - 1

        def top_stage(half, J):
            return J if half == 1 and 0 <= J < TOP_STAGES else None

        def top_bank(half, n):
            return x_ps[0][:, 0, :] if half == HALVES - 1 and n % 2 else top_ps[:]

        TOP_STAGES = 5

        @block.sync
        def _(sp):
            sp.dma_start(ids_sb[:], ids).then_inc(ids_in, 16)

            sp.dma_start(ident[:], ident_in).then_inc(ident_in_sb, 16)

            def load(c):
                if c >= 3:
                    sp.wait_ge(w_stacked[c - 3], STACK_INC)
                sp.dma_start(w_low[:, c % 3, :], w_nat[:, c * CR * P:(c + 1) * CR * P]).then_inc(w_in[c % 3], 16)

            def stack(c):
                sp.wait_ge(w_split, c + 1)
                for slot in range(4):
                    part = w_high[:, c % 2, :] if slot < 2 else w_low[:, c % 3, :]
                    for q in range(R):
                        sp.dma_start(w_stack[slot * E:(slot + 1) * E, q, c * CR:(c + 1) * CR, :].bitcast(fp32)
                                     .rearrange("e k c -> e (k c)"),
                                     part[q * E:(q + 1) * E, :]).then_inc(w_stacked[c], 16)

            load(0)
            load(1)
            for c in range(NC):
                stack(c)
                if c + 2 < NC:
                    load(c + 2)
                if c == 0:
                    for j in range(R):
                        sp.dma_start(wd_sb[j * E:(j + 1) * E].rearrange("p k d -> p (k d)"),
                                     w_dense[j:j + 1, :].to_broadcast([E, NBR * R * D])).then_inc(consts_in, 16)
            sp.wait_ge(memset_done, 1)
            for c in range(NC - 3, NC):
                sp.wait_ge(w_stacked[c], STACK_INC)
            for dst, src in ((sel[:], sel_in), (db_sb[:], dense_b), (gcol[0:D], gamma),
                             (bcol[0:D], beta), (w1_sb[:], w1), (b1_sb[:], b1),
                             (w2_sb, w2.rearrange("(k p) n -> p k n", p=P)), (b2_sb[:], b2),
                             (w3_sb[:], w3),
                             (cat[:, :, D:], ctx_in.rearrange("(t p) c -> p t c", p=P))):
                sp.dma_start(dst, src).then_inc(top_in, 16)
            for half in range(HALVES):
                sp.wait_ge(y_kept, half + 1)
                sp.dma_start(out[:, half * BH:(half + 1) * BH], y_sb[:]).then_inc(stored, 16)
            sp.wait_ge(stored, 16 * HALVES)

        @block.gpsimd
        def _(pool):
            pool.wait_ge(ids_in, 16)
            for g in range(NG):
                half, J = divmod(g, G)
                if g >= 3:
                    pool.wait_ge(x_split, g - 2)
                    pool.wait_ge(filled, FILLS * (g - 2))
                for t in range(TH):
                    for r in range(R):
                        f = J * R + r
                        pool.indirect_dma_start(
                            emb[:, g % 3, t, r, :], None, tables[f],
                            bass.IndirectOffsetOnAxis(ap=ids_sb[:, f, half * TH + t:half * TH + t + 1], axis=0),
                        ).then_inc(gathered[g], 16)

        @block.scalar
        def _(act):
            def double_group(g):
                if g >= 2:
                    act.wait_ge(filled, FILLS * (g - 1))
                parts = emb_parts[:, g % 2].rearrange("p t r o s e -> p (t r) o s e")
                high = emb_high[:].rearrange("p t r e -> p (t r) e")
                act.wait_ge(high_ready, g + 1)
                act.activation(parts[:, :, :, 0, :], high.unsqueeze(2).to_broadcast([P, TH * R, 2, E]),
                               ACT.Copy).then_inc(x_doubled, 1)
                act.wait_ge(x_split, g + 1)
                act.activation(parts[:, :, 1, 1, :], parts[:, :, 0, 1, :], ACT.Copy).then_inc(x_doubled, 1)

            def keep_fill(g, k):
                n = FILLS * g + k
                act.wait_ge(filled, n + 1)
                if k < FILLS - 1:
                    act.activation(x_stack[:, g % G, 2 * k:2 * k + 2, :], x_ps[n % 2][:], ACT.Copy).then_inc(kept, 1)
                else:
                    if g >= 3:
                        act.wait_ge(prod_ready, NBR * ((g - 3) // G) + ROWS_OF[(g - 3) % G] + (g - 3) % G + 1)
                    act.activation(xT[:, g % 3, :], x_ps[n % 2][:, 0, :], ACT.Copy).then_inc(kept, 1)

            def top(half, stage):
                if stage == 0:
                    act.wait_ge(summed, NBR * (half + 1))
                    for c in range(2):
                        act.activation(hT[c * E:c * E + D, :], hT_ps[c * E:c * E + D, half, :],
                                       ACT.Copy).then_inc(h_copied, 1)
                if stage == 1:
                    act.wait_ge(var_ready, half + 1)
                    act.activation(std[:], var[:], ACT.Sqrt, bias=eps[:], scale=1.0 / D).then_inc(std_ready, 1)
                if stage == 2:
                    act.wait_ge(cat_turned, half + 1)
                    if half == 0:
                        act.wait_ge(top_in, TOP)
                    act.activation(catT, top_ps[0:D + CTX, :], ACT.Identity, bias=bcol[:],
                                   scale=gcol[:]).then_inc(catT_ready, 1)
                if stage == 3:
                    for c in range(N1 // P):
                        act.wait_ge(l1_ready, N1 // P * half + c + 1)
                        act.activation(a1[:, c, :], top_bank(half, c), ACT.Relu, bias=b1_sb[:, c:c + 1]).then_inc(a1_ready, 1)
                if stage == 4:
                    for c in range(N2 // P):
                        act.wait_ge(l2_ready, N2 // P * half + c + 1)
                        act.activation(a2[:, c, :], top_bank(half, c), ACT.Relu, bias=b2_sb[:, c:c + 1]).then_inc(a2_ready, 1)
                    act.wait_ge(y_ready, half + 1)
                    if half == 1:
                        act.wait_ge(stored, 16)
                    act.activation(y_sb[:], top_ps[0:1, :], ACT.Copy).then_inc(y_kept, 1)

            act.wait_ge(memset_done, 1)
            act.activation(warm[:], eps[:], ACT.Sqrt)
            act.wait_ge(ident_in_sb, 16)
            act.activation(ident_r[:], ident[:], ACT.Copy).then_inc(ident_kept, 1)
            double_group(0)
            for k in range(FILLS):
                keep_fill(0, k)
            for g in range(NG):
                half, J = divmod(g, G)
                if g + 1 < NG:
                    double_group(g + 1)
                    for k in range(FILLS):
                        keep_fill(g + 1, k)
                if top_stage(half, J) is not None:
                    top(0, top_stage(half, J))
            for stage in range(TOP_STAGES):
                top(1, stage)

        @block.vector
        def _(dve):
            def split_chunk(c):
                dve.wait_ge(w_in[c % 3], 16 * (c // 3 + 1))
                if c >= 2:
                    dve.wait_ge(w_stacked[c - 2], STACK_INC)
                dve.tensor_scalar(w_high[:, c % 2, :].bitcast(u32), w_low[:, c % 3, :].bitcast(u32),
                                  HIGH_BITS, None, ALU.bitwise_and).then_inc(w_high_ready, 1)
                dve.wait_ge(w_high_ready, c + 1)
                dve.tensor_tensor(w_low[:, c % 3, :], w_low[:, c % 3, :], w_high[:, c % 2, :],
                                  ALU.subtract).then_inc(w_split, 1)

            def split_group(g):
                dve.wait_ge(gathered[g], 16 * R * TH)
                if g >= 1:
                    dve.wait_ge(x_doubled, 2 * g)
                    dve.wait_ge(x_split, g)
                if g >= 2:
                    dve.wait_ge(filled, FILLS * (g - 1))
                x = emb[:, g % 3].rearrange("p t r e -> p (t r) e")
                high = emb_high[:].rearrange("p t r e -> p (t r) e")
                parts = emb_parts[:, g % 2].rearrange("p t r o s e -> p (t r) o s e")
                dve.tensor_scalar(high.bitcast(u32), x.bitcast(u32), HIGH_BITS, None,
                                  ALU.bitwise_and).then_inc(high_ready, 1)
                dve.wait_ge(high_ready, g + 1)
                dve.tensor_tensor(parts[:, :, 0, 1, :], x, high, ALU.subtract).then_inc(x_split, 1)

            def top(half, stage):
                if stage == 0:
                    dve.wait_ge(summed, NBR * (half + 1))
                    for c in range(2, R):
                        dve.tensor_copy(hT[c * E:c * E + D, :], hT_ps[c * E:c * E + D, half, :]).then_inc(h_copied, 1)
                if stage == 1:
                    hb = top_ps[:, 0:TH * D].rearrange("p (t d) -> p t d", d=D)
                    dve.wait_ge(hb_ready, half + 1)
                    dve.tensor_reduce(total[:], hb, AX.X, ALU.add).then_inc(ln, 1)
                    dve.wait_ge(ln, 5 * half + 1)
                    dve.tensor_scalar(mean[:], total[:], 1.0 / D, None, ALU.mult).then_inc(ln, 1)
                    dve.wait_ge(ln, 5 * half + 2)
                    dve.tensor_tensor(h_sb[:], hb, mean[:].unsqueeze(2).to_broadcast([P, TH, D]),
                                      ALU.subtract).then_inc(ln, 1)
                    dve.wait_ge(ln, 5 * half + 3)
                    dve.tensor_tensor(sq[:], h_sb[:], h_sb[:], ALU.mult).then_inc(ln, 1)
                    dve.wait_ge(ln, 5 * half + 4)
                    dve.tensor_reduce(var[:], sq[:], AX.X, ALU.add).then_inc(var_ready, 1)
                    dve.wait_ge(std_ready, half + 1)
                    dve.reciprocal(rstd[:], std[:]).then_inc(ln, 1)
                    dve.wait_ge(ln, 5 * half + 5)
                    dve.tensor_tensor(cat[:, half * TH:(half + 1) * TH, 0:D], h_sb[:],
                                      rstd[:].unsqueeze(2).to_broadcast([P, TH, D]), ALU.mult).then_inc(cat_ready, 1)

            dve.memset(ones[:], 1.0)
            dve.memset(gcol[:], 1.0)
            dve.memset(bcol[:], 0.0)
            dve.memset(eps[:], LN_EPS).then_inc(memset_done, 1)
            for c in range(2):
                split_chunk(c)
            split_group(0)
            chunk = 2
            s = 0
            for g in range(NG):
                half, J = divmod(g, G)
                for I in range(J + 1):
                    if I == split_at(J) and g + 1 < NG:
                        split_group(g + 1)
                    dve.wait_ge(t_ready, s + 1)
                    if I == 0:
                        dve.wait_ge(kept, FILLS * (g + 1))
                    if s >= 2:
                        dve.wait_ge(summed, s - 1)
                    n = blocks(I, J)
                    dve.tensor_tensor(prod[:, s % 2, 0:n, :], t_ps[s % 2][:, 0:n, :],
                                      xT[:, g % 3:g % 3 + 1, :].to_broadcast([P, n, BH]), ALU.mult).then_inc(prod_ready, 1)
                    s += 1
                if chunk < NC:
                    split_chunk(chunk)
                    chunk += 1
                if g == G - 1:
                    dve.wait_ge(w_stacked[NC - 1], STACK_INC)
                    dve.wait_ge(w_stacked[NC - 2], STACK_INC)
                    dve.memset(hT, 0.0)
                if top_stage(half, J) is not None:
                    top(0, top_stage(half, J))
            for stage in range(TOP_STAGES):
                top(1, stage)

        @block.tensor
        def _(pe):
            def free_bank(n):
                if n >= 2:
                    pe.wait_ge(kept, n - 1)

            def fill(g, k):
                n = FILLS * g + k
                free_bank(n)
                pe.wait_ge(x_split, g + 1)
                pe.wait_ge(x_doubled, 2 * (g + 1))
                for t in range(TH):
                    cols = slice(t * P, (t + 1) * P)
                    if k < FILLS - 1:
                        for r in range(2):
                            last = pe.matmul(x_ps[n % 2][:, r, cols],
                                             emb_parts[:, g % 2, t, 2 * k + r].rearrange("p o s e -> p (o s e)"),
                                             ident_r[:], start=True, stop=True)
                    else:
                        last = pe.transpose(x_ps[n % 2][:, 0, cols],
                                            emb[:, g % 3, t].rearrange("p r e -> p (r e)"), ident[:])
                last.then_inc(filled, 1)

            def sum_step(s):
                half, row = divmod(s, NBR)
                pe.wait_ge(prod_ready, s + 1)
                if row == 0 and half > 0:
                    pe.wait_ge(h_copied, R * half)
                J = max(j for j in range(G) if ROWS_OF[j] <= row)
                for q in range(blocks(row - ROWS_OF[J], J)):
                    final = row == (NBR - 1 if q < R - 1 else NBR - 2)
                    last = pe.matmul(hT_ps[q * E:q * E + D, half, :], wd_sb[:, row * R + q, :], prod[:, s % 2, q, :],
                                     start=row == (0 if q < R - 1 else 1), stop=final)
                last.then_inc(summed, 1)

            def top(half, stage):
                if stage == 0:
                    if half == 0:
                        pe.wait_ge(top_in, TOP)
                    pe.wait_ge(h_copied, R * (half + 1))
                    for t in range(TH):
                        o = top_ps[:, t * D:(t + 1) * D]
                        pe.matmul(o, hT[:, t * P:(t + 1) * P], sel[:], start=True, stop=False)
                        last = pe.matmul(o, ones[:], db_sb[:], start=False, stop=True)
                    last.then_inc(hb_ready, 1)
                if stage == 2:
                    pe.wait_ge(cat_ready, half + 1)
                    for t in range(TH):
                        last = pe.transpose(top_ps[0:D + CTX, t * P:(t + 1) * P], cat[:, half * TH + t, :], ident[:])
                    last.then_inc(cat_turned, 1)
                if stage == 3:
                    pe.wait_ge(catT_ready, half + 1)
                    for c in range(N1 // P):
                        lag = 2 if half == HALVES - 1 else 1
                        if c >= lag:
                            pe.wait_ge(a1_ready, N1 // P * half + c - lag + 1)
                        pe.matmul(top_bank(half, c), w1_sb[:, c * P:(c + 1) * P], catT, start=True,
                                  stop=True).then_inc(l1_ready, 1)
                if stage == 4:
                    pe.wait_ge(a1_ready, N1 // P * (half + 1))
                    for c in range(N2 // P):
                        if c == 1 and half < HALVES - 1:
                            pe.wait_ge(a2_ready, N2 // P * half + 1)
                        for k in range(N1 // P):
                            last = pe.matmul(top_bank(half, c), w2_sb[:, k, c * P:(c + 1) * P], a1[:, k, :],
                                             start=k == 0, stop=k == N1 // P - 1)
                        last.then_inc(l2_ready, 1)
                    pe.wait_ge(a2_ready, N2 // P * (half + 1))
                    for k in range(N2 // P):
                        last = pe.matmul(top_ps[0:1, :], w3_sb[:, k:k + 1], a2[:, k, :], start=k == 0,
                                         stop=k == N2 // P - 1)
                    last.then_inc(y_ready, 1)

            pe.wait_ge(ident_kept, 1)
            for k in range(FILLS):
                fill(0, k)
            s = 0
            for g in range(NG):
                half, J = divmod(g, G)
                for I in range(J + 1):
                    for k in range(FILLS):
                        if I == fill_at(J, k) and g + 1 < NG:
                            fill(g + 1, k)
                    row = ROWS_OF[J] + I
                    if half == 0 and row % CR == 0:
                        pe.wait_ge(w_stacked[row // CR], STACK_INC)
                    if I == 0:
                        pe.wait_ge(kept, FILLS * (g + 1))
                    if s >= 2:
                        pe.wait_ge(prod_ready, s - 1)
                    for q in range(blocks(I, J)):
                        last = pe.matmul(t_ps[s % 2][:, q, :], w_stack[:, q, row, :], x_stack[:, I, q, :],
                                         start=True, stop=True)
                    last.then_inc(t_ready, 1)
                    if s == 1:
                        pe.wait_ge(consts_in, CONSTS)
                    if s >= 1:
                        sum_step(s - 1)
                    s += 1
                if top_stage(half, J) is not None:
                    top(0, top_stage(half, J))
            sum_step(NS - 1)
            for stage in range(TOP_STAGES):
                top(1, stage)


def kernel(**inputs):
    import concourse.bacc as bacc
    from concourse.bass_utils import run_bass_kernel_spmd

    a = {k: np.ascontiguousarray(v) for k, v in inputs.items()}
    arrays = {}
    arrays["ids"] = np.ascontiguousarray(a["ids"].reshape(BT, P, F).transpose(1, 2, 0).astype(np.int32, copy=False))
    for f in range(F):
        arrays[f"tbl_{f}"] = a[f"tbl_{f}"]
    pair = np.full((F, F), -1)
    pair[np.triu_indices(F, 1)] = np.arange(F * (F - 1) // 2)
    w_nat = np.zeros((R, E, NBR, R, E), a["L0_rec_W"].dtype)
    w_dense = np.zeros((R, NBR, R, D), a["L0_rec_dense_w"].dtype)
    for J in range(G):
        for I in range(J + 1):
            for q in range(R):
                for r in range(R):
                    p = pair[I * R + q, J * R + r]
                    if p >= 0:
                        w_nat[q, :, ROWS_OF[J] + I, r, :] = a["L0_rec_W"][p]
                        w_dense[r, ROWS_OF[J] + I, q, :] = a["L0_rec_dense_w"][p]
    arrays["w_nat"] = w_nat.reshape(P, NBR * P)
    arrays["w_dense"] = w_dense.reshape(R, NBR * R * D)
    arrays["dense_b"] = a["L0_rec_dense_b"].reshape(1, D)
    arrays["gamma"] = a["L0_rec_gamma"].reshape(D, 1)
    arrays["beta"] = a["L0_rec_beta"].reshape(D, 1)
    arrays["ctx_in"] = a["dense_ctx"]
    arrays["w1"] = a["W_top1"]
    arrays["b1"] = np.ascontiguousarray(a["b_top1"].reshape(N1 // P, P).T)
    arrays["w2"] = a["W_top2"]
    arrays["b2"] = np.ascontiguousarray(a["b_top2"].reshape(N2 // P, P).T)
    arrays["w3"] = np.ascontiguousarray(a["W_top3"].reshape(N2 // P, P).T)
    arrays["ident_in"] = np.eye(P, dtype=np.float32)
    arrays["sel_in"] = np.concatenate([np.eye(E, D, dtype=np.float32)] * R, axis=0)

    nc = bacc.Bacc("TRN2", target_bir_lowering=False, num_devices=1)
    ap = {n: nc.dram_tensor(n, v.shape, mybir.dt.from_np(v.dtype), kind="ExternalInput").ap() for n, v in arrays.items()}
    out = nc.dram_tensor("out", (B, 1), mybir.dt.float32, kind="ExternalOutput").ap()
    tables = [ap.pop(f"tbl_{f}") for f in range(F)]
    build(nc, tables=tables, out=out.rearrange("b o -> o b"), **ap)
    r = run_bass_kernel_spmd(nc, [arrays], core_ids=[0])
    return r.results[0]["out"]
```

```python
import numpy as np
import concourse.bass as bass
from concourse import mybir
from contextlib import ExitStack

B, F, E, D = 512, 40, 32, 16
CTX = 16
N1, N2 = 512, 256
LN_EPS = 0.001
P = 128
BT = B // P
R = P // E
G = F // R
ROWS_OF = [sum(range(1, j + 1)) for j in range(G)]
NBR = G * (G + 1) // 2
HALVES = 2
BH = B // HALVES
TH = BH // P
CR = 4
NC = -(-NBR // CR)
RAW = 4
PRODS = 3
LAG = 2
RING = 6
XT = 4
HIGH_BITS = 0xFFFFF000


def build(nc, ids, tables, w_nat, w_dense, dense_b, gamma, beta, ctx_in, w1, b1, w2, b2, w3,
          ident_in, sel_in, out):
    fp32, f32r, i32, u32 = mybir.dt.float32, mybir.dt.float32r, mybir.dt.int32, mybir.dt.uint32
    ALU, ACT, AX = mybir.AluOpType, mybir.ActivationFunctionType, mybir.AxisListType

    with ExitStack() as ctx:
        def sb(name, shape, dt=fp32):
            return ctx.enter_context(nc.sbuf_tensor(name, shape, dt))

        def psum(name, shape, dt=fp32):
            return ctx.enter_context(nc.psum_tensor(name, shape, dt))

        def sem(name):
            return ctx.enter_context(nc.semaphore(name))

        w_stack = sb("w_stack", [P, R, NBR, P], f32r)
        x_stack = sb("x_stack", [P, G, R, BH], f32r)
        xT = sb("xT", [P, XT, BH])
        emb = sb("emb", [P, RING, TH, R, E])
        emb_high = sb("emb_high", [P, TH, R, E])
        emb_parts = sb("emb_parts", [P, TH, R, 2, E], f32r)
        wd_sb = sb("wd_sb", [P, NBR * R, D])
        prod = sb("prod", [P, PRODS, R, BH])
        ids_sb = sb("ids_sb", [P, F, BT], i32)
        ident_r = sb("ident_r", [P, P], f32r)
        spread = sb("spread", [P, 4 * R + 2, E], f32r)
        ident_raw = emb_high[:].rearrange("p t r e -> p (t r e)")[:, 0:P]
        ident = ident_r[:].bitcast(fp32)
        early = sb("early", [P, (RAW + 2) * CR * P])
        w_raw = early[:, 0:RAW * CR * P].rearrange("p (u c) -> p u c", u=RAW)
        w_high = early[:, RAW * CR * P:].rearrange("p (u c) -> p u c", u=2)
        w_parts = x_stack[:, G - 2:G].rearrange("p j q b -> p (j q b)").rearrange("p (s u c) -> p s u c", s=2, u=2)
        w_high_r, w_low_r = w_parts[:, 0], w_parts[:, 1]
        w2_sb = early[:, 0:N1 // P * N2].rearrange("p (k n) -> p k n", n=N2)
        a1_first = early[:, N1 // P * N2:N1 // P * (N2 + BH)].rearrange("p (k b) -> p k b", b=BH)
        a2 = early[:, N1 // P * (N2 + BH):N1 // P * (N2 + BH) + N2 // P * BH].rearrange("p (k b) -> p k b", b=BH)
        a1 = [a1_first, prod[:, 0]]
        y_sb = prod[0:1, 1, 0:HALVES, :]
        hT = early[:, 5 * CR * P:5 * CR * P + BH]
        catT = early[0:D + CTX, 5 * CR * P + BH:5 * CR * P + 2 * BH]
        w1_sb = sb("w1_sb", [D + CTX, N1])
        sel = sb("sel", [P, D])
        db_sb = sb("db_sb", [P, 1])
        gcol = sb("gcol", [D + CTX, 1])
        bcol = sb("bcol", [D + CTX, 1])
        b1_sb = sb("b1_sb", [P, N1 // P])
        b2_sb = sb("b2_sb", [P, N2 // P])
        w3_sb = sb("w3_sb", [P, N2 // P])
        h_sb = sb("h_sb", [P, TH, D])
        sq = sb("sq", [P, TH, D])
        var = sb("var", [P, TH])
        std = sb("std", [P, TH])
        rstd = sb("rstd", [P, TH])
        eps = sb("eps", [P, 1])
        cat = sb("cat", [P, BT, D + CTX])

        t_ps = [psum(f"t_ps{i}", [P, R, BH]) for i in range(2)]
        hT_ps = psum("hT_ps", [P, HALVES, BH])
        x_ps = [psum(f"x_ps{i}", [P, 2, BH]) for i in range(2)]
        top_ps = psum("top_ps", [P, BH])

        ids_in = sem("ids_in")
        gathered = [sem(f"gathered{g}") for g in range(HALVES * G)]
        w_in = [sem(f"w_in{i}") for i in range(RAW)]
        w_high_ready = sem("w_high_ready")
        w_split = sem("w_split")
        w_high_kept = sem("w_high_kept")
        w_spread = sem("w_spread")
        w_kept = {e: sem(f"w_kept_{e}") for e in ("act", "dve")}
        ident_kept = sem("ident_kept")
        ident_in_sb = sem("ident_in_sb")
        consts_in = sem("consts_in")
        top_in = sem("top_in")
        memset_done = sem("memset_done")
        high_ready = sem("high_ready")
        x_split = sem("x_split")
        high_kept = sem("high_kept")
        turned = sem("turned")
        xT_kept = sem("xT_kept")
        spread_x = sem("spread_x")
        x_kept = sem("x_kept")
        t_ready = sem("t_ready")
        prod_ready = sem("prod_ready")
        summed = sem("summed")
        h_copied = sem("h_copied")
        centred_ready = sem("centred_ready")
        ln = sem("ln")
        var_ready = sem("var_ready")
        std_ready = sem("std_ready")
        cat_ready = sem("cat_ready")
        cat_turned = sem("cat_turned")
        catT_ready = sem("catT_ready")
        l1_ready = sem("l1_ready")
        a1_ready = sem("a1_ready")
        l2_ready = sem("l2_ready")
        a2_ready = sem("a2_ready")
        y_ready = sem("y_ready")
        y_kept = sem("y_kept")
        stored = sem("stored")

        block = ctx.enter_context(nc.Block())

        NG = HALVES * G
        NS = HALVES * NBR

        ORDER = [(half, J, I) for half in range(HALVES) for J in range(G) for I in range(J + 1)]
        FIRST = [ORDER.index((g // G, g % G, 0)) for g in range(NG)]
        LAST = [ORDER.index((g // G, g % G, g % G)) for g in range(NG)]
        HALF_END = [LAST[G - 1], LAST[NG - 1]]

        AHEAD = 3
        TURN_AT, SPLIT_AT, SPREAD_AT = {}, {}, {}
        for g in range(AHEAD, NG):
            waits = g > G + 2
            TURN_AT[g] = FIRST[g] - (0 if waits else 2)
            SPLIT_AT[g] = max(LAST[g] - 5, FIRST[g]) if waits else LAST[g] - 5
            SPREAD_AT[g] = SPLIT_AT[g] + 1

        def groups_at(steps, s):
            return [g for g in range(AHEAD, NG) if s == steps[g]]

        def split_after_chunk(c):
            return [g for g in range(AHEAD) if c == 4 * (g + 1)]

        def spread_after_chunk(c):
            return [g for g in range(AHEAD) if c == min(4 * (g + 1) + 1, NC - 1)]

        KEPT = 4

        def chunk_rows(c):
            return min(CR, NBR - c * CR)

        def copier(c, q):
            return "act" if q < 2 or (q == 2 and c % 2 == 0) else "dve"

        def copied(engine, c, q):
            return sum(copier(*x) == engine for x in ((d, p) for d in range(c + 1) for p in range(R)) if x <= (c, q))

        def w_bank(q):
            return t_ps[q // 2][:, 2 * (q % 2):2 * (q % 2) + 2, :].rearrange("p a b -> p (a b)")

        def keep_spread(c, engine, copy):
            for q in range(R):
                if copier(c, q) == engine:
                    cols = chunk_rows(c) * P
                    copy(w_stack[:, q, c * CR:c * CR + chunk_rows(c), :].rearrange("p k c -> p (k c)"),
                         w_bank(q)[:, 0:cols], R * c + q + 1)

        CONSTS = 16 * R
        TOP = 16 * 10

        def blocks(I, J):
            return R if I < J else R - 1

        LN = 3
        L1, L2 = N1 // P, N2 // P
        PAUSE, EVERY, MID = 8, 4, L1
        NORMALISE = [("sums",), ("center",), ("variance",), ("scale",), ("turn",)]
        LAYER1 = [("layer1", c) for c in range(L1)]
        LAYER2 = [("layer2", c, k) for c in range(L2) for k in range(L1)]
        BETWEEN, AFTER = LAYER1 + LAYER2[:MID], LAYER2[MID:]
        PIECES_AFTER = {HALF_END[0] + LAG + n: piece for n, piece in enumerate(NORMALISE)}
        PIECES_AFTER |= {HALF_END[0] + LAG + len(NORMALISE) + PAUSE + EVERY * c: piece for c, piece in enumerate(BETWEEN)}

        def pieces_after(s):
            return [PIECES_AFTER[s]] if s in PIECES_AFTER else []

        END = ([(1, "sums")] + [(0, *p) for p in AFTER[:1]] + [(1, "center")] + [(0, *p) for p in AFTER[1:2]] +
               [(1, "variance")] + [(0, *p) for p in AFTER[2:]] + [(1, "scale"), (1, "turn")] +
               [(0, "layer3")] + [(1, *p) for p in LAYER1 + LAYER2] + [(1, "layer3")])

        def layer1_bank(half, c):
            return top_ps[:] if half == 0 else t_ps[c // 2][:, 2 * (c % 2), :]

        def layer2_bank(half, c):
            return top_ps[:] if half == 0 and c == 0 else x_ps[c][:, 0, :]

        def y_bank(half):
            return hT_ps[0:1, 0, :] if half == 0 else top_ps[0:1, :]

        @block.sync
        def _(sp):
            sp.dma_start(ids_sb[:], ids).then_inc(ids_in, 16)
            sp.dma_start(ident_raw, ident_in).then_inc(ident_in_sb, 16)
            for c in range(NC):
                if c >= RAW:
                    sp.wait_ge(w_split, c - RAW + 1)
                sp.dma_start(w_raw[:, c % RAW, 0:chunk_rows(c) * P],
                             w_nat[:, c * CR * P:(c * CR + chunk_rows(c)) * P]).then_inc(w_in[c % RAW], 16)
            for j in range(R):
                sp.dma_start(wd_sb[j * E:(j + 1) * E].rearrange("p k d -> p (k d)"),
                             w_dense[j:j + 1, :].to_broadcast([E, NBR * R * D])).then_inc(consts_in, 16)
            sp.wait_ge(memset_done, 1)
            sp.wait_ge(w_split, NC)
            for dst, src in ((sel[:], sel_in), (db_sb[0:D], dense_b), (gcol[0:D], gamma),
                             (bcol[0:D], beta), (w1_sb[:], w1), (b1_sb[:], b1),
                             (w2_sb, w2.rearrange("(k p) n -> p k n", p=P)), (b2_sb[:], b2),
                             (w3_sb[:], w3),
                             (cat[:, :, D:], ctx_in.rearrange("(t p) c -> p t c", p=P))):
                sp.dma_start(dst, src).then_inc(top_in, 16)
            sp.wait_ge(y_kept, HALVES)
            sp.dma_start(out, y_sb.rearrange("p h b -> p (h b)")).then_inc(stored, 16)
            sp.wait_ge(stored, 16)

        @block.gpsimd
        def _(pool):
            pool.wait_ge(ids_in, 16)
            for g in range(NG):
                half, J = divmod(g, G)
                if g >= RING:
                    pool.wait_ge(x_split, g - RING + 1)
                    pool.wait_ge(turned, g - RING + 1)
                for t in range(TH):
                    for r in range(R):
                        f = J * R + r
                        pool.indirect_dma_start(
                            emb[:, g % RING, t, r, :], None, tables[f],
                            bass.IndirectOffsetOnAxis(ap=ids_sb[:, f, half * TH + t:half * TH + t + 1], axis=0),
                        ).then_inc(gathered[g], 16)

        @block.scalar
        def _(act):
            def keep_high(g):
                act.wait_ge(high_ready, g + 1)
                if g >= 1:
                    act.wait_ge(spread_x, g)
                act.activation(emb_parts[:, :, :, 0, :], emb_high[:], ACT.Copy).then_inc(high_kept, 1)

            def keep_parts(g):
                act.wait_ge(spread_x, g + 1)
                for u in range(2):
                    for place in range(2):
                        act.activation(x_stack[place * 2 * E:(place + 1) * 2 * E, g % G, u::2, :],
                                       x_ps[0][u * 2 * E:(u + 1) * 2 * E], ACT.Copy).then_inc(x_kept, 1)

            def keep_xT(g):
                act.wait_ge(turned, g + 1)
                if g >= XT:
                    act.wait_ge(prod_ready, LAST[g - XT] + 1)
                act.activation(xT[:, g % XT, :], x_ps[1][:, 0, :], ACT.Copy).then_inc(xT_kept, 1)

            def top(half, piece, c=0, k=0):
                if piece == "variance":
                    act.wait_ge(var_ready, half + 1)
                    act.activation(std[:], var[:], ACT.Sqrt, bias=eps[:], scale=1.0 / D).then_inc(std_ready, 1)
                if piece == "turn":
                    act.wait_ge(cat_turned, half + 1)
                    if half == 0:
                        act.wait_ge(top_in, TOP)
                    act.activation(catT, top_ps[0:D + CTX, :], ACT.Identity, bias=bcol[:],
                                   scale=gcol[:]).then_inc(catT_ready, 1)
                if piece == "layer1":
                    act.wait_ge(l1_ready, L1 * half + c + 1)
                    act.activation(a1[half][:, c, :], layer1_bank(half, c), ACT.Relu, bias=b1_sb[:, c:c + 1]).then_inc(a1_ready, 1)
                if piece == "layer2" and k == L1 - 1:
                    act.wait_ge(l2_ready, L2 * half + c + 1)
                    act.activation(a2[:, c, :], layer2_bank(half, c), ACT.Relu, bias=b2_sb[:, c:c + 1]).then_inc(a2_ready, 1)
                if piece == "layer3":
                    act.wait_ge(y_ready, half + 1)
                    act.activation(y_sb[:, half, :], y_bank(half), ACT.Copy).then_inc(y_kept, 1)

            act.wait_ge(memset_done, 1)
            act.activation(std[:, 0:1], eps[:], ACT.Sqrt)
            act.wait_ge(ident_in_sb, 16)
            act.activation(ident_r[:], ident_raw, ACT.Copy).then_inc(ident_kept, 1)
            for q in range(R):
                rows = slice(q * E, (q + 1) * E)
                act.activation(spread[rows, 4 * q + 2:4 * q + 4, :], ident_raw[rows, rows].unsqueeze(1).to_broadcast([E, 2, E]),
                               ACT.Copy).then_inc(ident_kept, 1)

            def keep_w_high(c):
                act.wait_ge(w_high_ready, c + 1)
                if c >= 2:
                    act.wait_ge(w_spread, R * (c - 1))
                cols = slice(0, chunk_rows(c) * P)
                act.activation(w_high_r[:, c % 2, cols], w_high[:, c % 2, cols], ACT.Copy).then_inc(w_high_kept, 1)

            def copy_w(dst, src, spread_count):
                act.wait_ge(w_spread, spread_count)
                act.activation(dst, src, ACT.Copy).then_inc(w_kept["act"], 1)

            keep_w_high(0)
            for c in range(NC):
                if c + 1 < NC:
                    keep_w_high(c + 1)
                keep_spread(c, "act", copy_w)
                for g in spread_after_chunk(c):
                    keep_xT(g)
                    keep_parts(g)
                for g in split_after_chunk(c):
                    keep_high(g)
            for s in range(NS):
                for g in groups_at(TURN_AT, s):
                    keep_xT(g)
                for g in groups_at(SPREAD_AT, s):
                    keep_parts(g)
                for g in groups_at(SPLIT_AT, s):
                    keep_high(g)
                for piece in pieces_after(s):
                    top(0, *piece)
            for half, *piece in END:
                top(half, *piece)

        @block.vector
        def _(dve):
            def split_chunk(c):
                cols = slice(0, chunk_rows(c) * P)
                dve.wait_ge(w_in[c % RAW], 16 * (c // RAW + 1))
                if c >= 2:
                    dve.wait_ge(w_high_kept, c - 1)
                    dve.wait_ge(w_split, c - 1)
                dve.tensor_scalar(w_high[:, c % 2, cols].bitcast(u32), w_raw[:, c % RAW, cols].bitcast(u32),
                                  HIGH_BITS, None, ALU.bitwise_and).then_inc(w_high_ready, 1)
                dve.wait_ge(w_high_ready, c + 1)
                if c >= 2:
                    dve.wait_ge(w_spread, R * (c - 1))
                dve.tensor_tensor(w_low_r[:, c % 2, cols], w_raw[:, c % RAW, cols], w_high[:, c % 2, cols],
                                  ALU.subtract).then_inc(w_split, 1)

            def copy_w(dst, src, spread_count):
                dve.wait_ge(w_spread, spread_count)
                dve.tensor_copy(dst, src).then_inc(w_kept["dve"], 1)

            def split_group(g):
                dve.wait_ge(gathered[g], 16 * R * TH)
                if g >= 1:
                    dve.wait_ge(high_kept, g)
                    dve.wait_ge(x_split, g)
                    dve.wait_ge(spread_x, g)
                x = emb[:, g % RING].rearrange("p t r e -> p (t r) e")
                high = emb_high[:].rearrange("p t r e -> p (t r) e")
                parts = emb_parts[:].rearrange("p t r s e -> p (t r) s e")
                dve.tensor_scalar(high.bitcast(u32), x.bitcast(u32), HIGH_BITS, None,
                                  ALU.bitwise_and).then_inc(high_ready, 1)
                dve.wait_ge(high_ready, g + 1)
                dve.tensor_tensor(parts[:, :, 1, :], x, high, ALU.subtract).then_inc(x_split, 1)

            def top(half, piece, c=0, k=0):
                if piece == "sums":
                    dve.wait_ge(summed, HALF_END[half] + 1)
                    if half == 0:
                        dve.wait_ge(top_in, TOP)
                    dve.tensor_scalar(hT, hT_ps[:, half, :], db_sb[:], None, ALU.add).then_inc(h_copied, 1)
                if piece == "variance":
                    centred = top_ps[:, 0:TH * D].rearrange("p (t d) -> p t d", d=D)
                    dve.wait_ge(centred_ready, half + 1)
                    dve.tensor_copy(h_sb[:], centred).then_inc(ln, 1)
                    dve.wait_ge(ln, LN * half + 1)
                    dve.tensor_tensor(sq[:], h_sb[:], h_sb[:], ALU.mult).then_inc(ln, 1)
                    dve.wait_ge(ln, LN * half + 2)
                    dve.tensor_reduce(var[:], sq[:], AX.X, ALU.add).then_inc(var_ready, 1)
                if piece == "scale":
                    dve.wait_ge(std_ready, half + 1)
                    dve.reciprocal(rstd[:], std[:]).then_inc(ln, 1)
                    dve.wait_ge(ln, LN * half + LN)
                    dve.tensor_tensor(cat[:, half * TH:(half + 1) * TH, 0:D], h_sb[:],
                                      rstd[:].unsqueeze(2).to_broadcast([P, TH, D]), ALU.mult).then_inc(cat_ready, 1)

            dve.memset(spread[:].bitcast(fp32), 0.0)
            dve.memset(hT_ps[:], 0.0)
            dve.memset(db_sb[:], 0.0)
            dve.memset(gcol[:], 1.0)
            dve.memset(bcol[:], 0.0)
            dve.memset(eps[:], LN_EPS).then_inc(memset_done, 1)
            split_chunk(0)
            for c in range(NC):
                if c + 1 < NC:
                    split_chunk(c + 1)
                keep_spread(c, "dve", copy_w)
                for g in split_after_chunk(c):
                    split_group(g)
            for s, (half, J, I) in enumerate(ORDER):
                g = half * G + J
                for ahead in groups_at(SPLIT_AT, s):
                    split_group(ahead)
                dve.wait_ge(t_ready, s + 1)
                if I == 0:
                    dve.wait_ge(xT_kept, g + 1)
                if s >= PRODS:
                    dve.wait_ge(summed, s - PRODS + 1)
                n = blocks(I, J)
                dve.tensor_tensor(prod[:, s % PRODS, 0:n, :], t_ps[s % 2][:, 0:n, :],
                                  xT[:, g % XT:g % XT + 1, :].to_broadcast([P, n, BH]), ALU.mult).then_inc(prod_ready, 1)
                for piece in pieces_after(s):
                    top(0, *piece)
            for half, *piece in END:
                top(half, *piece)

        @block.tensor
        def _(pe):
            def turn(g):
                pe.wait_ge(gathered[g], 16 * R * TH)
                if g >= 1:
                    pe.wait_ge(xT_kept, g)
                for t in range(TH):
                    last = pe.transpose(x_ps[1][:, 0, t * P:(t + 1) * P],
                                        emb[:, g % RING, t].rearrange("p r e -> p (r e)"), ident)
                last.then_inc(turned, 1)

            def spread_parts(g):
                pe.wait_ge(x_split, g + 1)
                pe.wait_ge(high_kept, g + 1)
                if g >= 1:
                    pe.wait_ge(x_kept, KEPT * g)
                for t in range(TH):
                    for r in range(0, R, 2):
                        last = pe.matmul(x_ps[0][:, r // 2, t * P:(t + 1) * P],
                                         emb_parts[:, t, r:r + 2].rearrange("p r s e -> p (r s e)"),
                                         ident_r[:], start=True, stop=True)
                last.then_inc(spread_x, 1)

            def sum_step(s):
                half, J, I = ORDER[s]
                row = ROWS_OF[J] + I
                pe.wait_ge(prod_ready, s + 1)
                if s == HALF_END[0] + 1:
                    pe.wait_ge(h_copied, 1)
                for q in range(blocks(I, J)):
                    last = pe.matmul(hT_ps[q * E:q * E + D, half, :], wd_sb[:, row * R + q, :], prod[:, s % PRODS, q, :],
                                     start=row == (0 if q < R - 1 else 1), stop=row == (NBR - 1 if q < R - 1 else NBR - 2))
                last.then_inc(summed, 1)

            def top(half, piece, c=0, k=0):
                if piece == "center":
                    pe.wait_ge(h_copied, half + 1)
                    if half > 0:
                        pe.wait_ge(a2_ready, 1)
                    for t in range(TH):
                        last = pe.matmul(top_ps[:, t * D:(t + 1) * D], hT[:, t * P:(t + 1) * P], sel[:], start=True,
                                         stop=True)
                    last.then_inc(centred_ready, 1)
                if piece == "turn":
                    pe.wait_ge(cat_ready, half + 1)
                    for t in range(TH):
                        last = pe.transpose(top_ps[0:D + CTX, t * P:(t + 1) * P], cat[:, half * TH + t, :], ident)
                    last.then_inc(cat_turned, 1)
                if piece == "layer1":
                    if c == 0:
                        pe.wait_ge(catT_ready, half + 1)
                    elif half == 0:
                        pe.wait_ge(a1_ready, c)
                    pe.matmul(layer1_bank(half, c), w1_sb[:, c * P:(c + 1) * P], catT, start=True,
                              stop=True).then_inc(l1_ready, 1)
                if piece == "layer2":
                    if c == 0:
                        pe.wait_ge(a1_ready, L1 * half + (k if half else L1 - 1) + 1)
                    if k == 0 and half > 0:
                        pe.wait_ge(a2_ready, c + 1)
                    last = pe.matmul(layer2_bank(half, c), w2_sb[:, k, c * P:(c + 1) * P], a1[half][:, k, :],
                                     start=k == 0, stop=k == L1 - 1)
                    if k == L1 - 1:
                        last.then_inc(l2_ready, 1)
                if piece == "layer3":
                    for k in range(L2):
                        pe.wait_ge(a2_ready, L2 * half + k + 1)
                        last = pe.matmul(y_bank(half), w3_sb[:, k:k + 1], a2[:, k, :], start=k == 0,
                                         stop=k == L2 - 1)
                    last.then_inc(y_ready, 1)

            pe.wait_ge(ident_kept, 1 + R)
            for c in range(NC):
                cols = slice(0, chunk_rows(c) * P)
                pe.wait_ge(w_high_kept, c + 1)
                pe.wait_ge(w_split, c + 1)
                for q in range(R):
                    if c >= 1:
                        e = copier(c - 1, q)
                        pe.wait_ge(w_kept[e], copied(e, c - 1, q))
                    pe.matmul(w_bank(q)[:, cols], spread[:, 4 * q + 2:4 * q + 6, :].rearrange("p s e -> p (s e)"),
                              w_high_r[:, c % 2, cols], start=True, stop=False)
                    pe.matmul(w_bank(q)[:, cols], spread[:, 4 * q:4 * q + 4, :].rearrange("p s e -> p (s e)"),
                              w_low_r[:, c % 2, cols], start=False, stop=True).then_inc(w_spread, 1)
                for g in spread_after_chunk(c):
                    turn(g)
                    spread_parts(g)
            for e in w_kept:
                pe.wait_ge(w_kept[e], copied(e, NC - 1, R - 1))
            for s, (half, J, I) in enumerate(ORDER):
                for g in groups_at(TURN_AT, s):
                    turn(g)
                for g in groups_at(SPREAD_AT, s):
                    spread_parts(g)
                row = ROWS_OF[J] + I
                if I == J:
                    pe.wait_ge(x_kept, KEPT * (half * G + J + 1))
                if s >= 2:
                    pe.wait_ge(prod_ready, s - 1)
                for q in range(blocks(I, J)):
                    last = pe.matmul(t_ps[s % 2][:, q, :], w_stack[:, q, row, :], x_stack[:, I, q, :],
                                     start=True, stop=True)
                last.then_inc(t_ready, 1)
                if s == LAG:
                    pe.wait_ge(consts_in, CONSTS)
                if s >= LAG:
                    sum_step(s - LAG)
                for piece in pieces_after(s):
                    top(0, *piece)
            for s in range(NS - LAG, NS):
                sum_step(s)
            for half, *piece in END:
                top(half, *piece)


def kernel(**inputs):
    import concourse.bacc as bacc
    from concourse.bass_utils import run_bass_kernel_spmd

    a = {k: np.ascontiguousarray(v) for k, v in inputs.items()}
    arrays = {}
    arrays["ids"] = np.ascontiguousarray(a["ids"].reshape(BT, P, F).transpose(1, 2, 0))
    for f in range(F):
        arrays[f"tbl_{f}"] = a[f"tbl_{f}"]
    pair = np.full((F, F), -1)
    pair[np.triu_indices(F, 1)] = np.arange(F * (F - 1) // 2)
    w_nat = np.zeros((R, E, NBR, R, E), a["L0_rec_W"].dtype)
    w_dense = np.zeros((R, NBR, R, D), a["L0_rec_dense_w"].dtype)
    for J in range(G):
        for I in range(J + 1):
            for q in range(R):
                for r in range(R):
                    p = pair[I * R + q, J * R + r]
                    if p >= 0:
                        w_nat[q, :, ROWS_OF[J] + I, r, :] = a["L0_rec_W"][p]
                        w_dense[r, ROWS_OF[J] + I, q, :] = a["L0_rec_dense_w"][p]
    arrays["w_nat"] = w_nat.reshape(P, NBR * P)
    arrays["w_dense"] = w_dense.reshape(R, NBR * R * D)
    arrays["dense_b"] = a["L0_rec_dense_b"].reshape(D, 1)
    arrays["gamma"] = a["L0_rec_gamma"].reshape(D, 1)
    arrays["beta"] = a["L0_rec_beta"].reshape(D, 1)
    arrays["ctx_in"] = a["dense_ctx"]
    arrays["w1"] = a["W_top1"]
    arrays["b1"] = np.ascontiguousarray(a["b_top1"].reshape(N1 // P, P).T)
    arrays["w2"] = a["W_top2"]
    arrays["b2"] = np.ascontiguousarray(a["b_top2"].reshape(N2 // P, P).T)
    arrays["w3"] = np.ascontiguousarray(a["W_top3"].reshape(N2 // P, P).T)
    arrays["ident_in"] = np.eye(P, dtype=np.float32)
    arrays["sel_in"] = np.concatenate([np.eye(E, D, dtype=np.float32) -
                                       np.where(np.arange(E)[:, None] < D, np.float32(1 / D), np.float32(0))] * R, axis=0)

    nc = bacc.Bacc("TRN2", target_bir_lowering=False, num_devices=1)
    ap = {n: nc.dram_tensor(n, v.shape, mybir.dt.from_np(v.dtype), kind="ExternalInput").ap() for n, v in arrays.items()}
    out = nc.dram_tensor("out", (B, 1), mybir.dt.float32, kind="ExternalOutput").ap()
    tables = [ap.pop(f"tbl_{f}") for f in range(F)]
    build(nc, tables=tables, out=out.rearrange("b o -> o b"), **ap)
    r = run_bass_kernel_spmd(nc, [arrays], core_ids=[0])
    return r.results[0]["out"]
```
